# Optimizing a Trainium2 kernel written in Bass

```python
import numpy as np
import jax
import jax.numpy as jnp

def _softmax(x, axis=-1):
    return jax.nn.softmax(x, axis=axis)
def _gelu(x):
    return jax.nn.gelu(x, approximate=True)
def _silu(x):
    return jax.nn.silu(x)
def _sigmoid(x):
    return jax.nn.sigmoid(x)
def _layernorm(x, axis=-1, eps=1e-5):
    m = jnp.mean(x, axis=axis, keepdims=True)
    v = jnp.var(x, axis=axis, keepdims=True)
    return (x - m) / jnp.sqrt(v + eps)
def _scatter_add(tgt, idx, src, axis=0):
    return tgt.at[idx].add(src)
def _segment_sum(src, seg, n):
    return jax.ops.segment_sum(src, seg, n)

kernel_name = 'mk_conv_seq_d1_conv_nhwc768_943412'

def setup_inputs(seed: int = 0):
    np.random.seed(seed)
    _w = jnp.asarray
    def _rec_inputs():
        import jax
        import jax.numpy as jnp
        _gk = jax.random.key(seed)
        x = -4.65e-05 + 0.9999 * jax.random.normal(jax.random.fold_in(_gk, 1), (2, 128, 256, 768), jnp.float32)
        return x
    x = _rec_inputs()
    def _L0_conv_setup():
        import jax, jax.numpy as jnp
        import numpy as np
        DIM = 768
        N_BLOCKS = 8
        BLOCK = DIM // N_BLOCKS
        HIDDEN = BLOCK * 1
        LAMBDA = 0.01

        def _softshrink(x, lam):
            return jnp.sign(x) * jnp.maximum(jnp.abs(x) - lam, 0.0)
        key = jax.random.key(seed)
        ks = jax.random.split(key, 5)
        B, H, W = (2, 128, 256)
        x = jax.random.normal(ks[0], (B, H, W, DIM), dtype=jnp.float32)
        std = 0.02
        w1r = std * jax.random.truncated_normal(ks[1], -2.0, 2.0, (N_BLOCKS, BLOCK, HIDDEN), jnp.float32)
        w1i = std * jax.random.truncated_normal(ks[2], -2.0, 2.0, (N_BLOCKS, BLOCK, HIDDEN), jnp.float32)
        w2r = std * jax.random.truncated_normal(ks[3], -2.0, 2.0, (N_BLOCKS, HIDDEN, BLOCK), jnp.float32)
        w2i = std * jax.random.truncated_normal(ks[4], -2.0, 2.0, (N_BLOCKS, HIDDEN, BLOCK), jnp.float32)
        b1r = jnp.zeros((N_BLOCKS, HIDDEN), jnp.float32)
        b1i = jnp.zeros((N_BLOCKS, HIDDEN), jnp.float32)
        b2r = jnp.zeros((N_BLOCKS, BLOCK), jnp.float32)
        b2i = jnp.zeros((N_BLOCKS, BLOCK), jnp.float32)
        return {'x': x, 'w1r': w1r, 'w1i': w1i, 'b1r': b1r, 'b1i': b1i, 'w2r': w2r, 'w2i': w2i, 'b2r': b2r, 'b2i': b2i}
    _L0_conv_all = _L0_conv_setup()
    _L0_conv_in = {k: v for k, v in _L0_conv_all.items() if k in ('w1r', 'w1i', 'b1r', 'b1i', 'w2r', 'w2i', 'b2r', 'b2i', )}
    del _L0_conv_all

    return {
        "x": x,
        "L0_conv_w1r": _L0_conv_in["w1r"],
        "L0_conv_w1i": _L0_conv_in["w1i"],
        "L0_conv_b1r": _L0_conv_in["b1r"],
        "L0_conv_b1i": _L0_conv_in["b1i"],
        "L0_conv_w2r": _L0_conv_in["w2r"],
        "L0_conv_w2i": _L0_conv_in["w2i"],
        "L0_conv_b2r": _L0_conv_in["b2r"],
        "L0_conv_b2i": _L0_conv_in["b2i"],
    }

def reference(x, L0_conv_w1r, L0_conv_w1i, L0_conv_b1r, L0_conv_b1i, L0_conv_w2r, L0_conv_w2i, L0_conv_b2r, L0_conv_b2i):
    import jax
    import jax.numpy as jnp
    def _L0_conv_ref(x, w1r, w1i, b1r, b1i, w2r, w2i, b2r, b2i):
        import jax, jax.numpy as jnp
        import numpy as np
        DIM = 768
        N_BLOCKS = 8
        BLOCK = DIM // N_BLOCKS
        HIDDEN = BLOCK * 1
        LAMBDA = 0.01

        def _softshrink(x, lam):
            return jnp.sign(x) * jnp.maximum(jnp.abs(x) - lam, 0.0)
        B, H, W, D = x.shape
        residual = x
        xf = jnp.fft.rfft2(x, axes=(1, 2), norm='ortho')
        xf = xf.reshape(B, H, W // 2 + 1, N_BLOCKS, BLOCK)
        xr, xi = (jnp.real(xf), jnp.imag(xf))
        o1r = jnp.einsum('bhwns,nse->bhwne', xr, w1r) - jnp.einsum('bhwns,nse->bhwne', xi, w1i) + b1r
        o1i = jnp.einsum('bhwns,nse->bhwne', xr, w1i) + jnp.einsum('bhwns,nse->bhwne', xi, w1r) + b1i
        o1r = jax.nn.relu(o1r)
        o1i = jax.nn.relu(o1i)
        o2r = jnp.einsum('bhwne,nes->bhwns', o1r, w2r) - jnp.einsum('bhwne,nes->bhwns', o1i, w2i) + b2r
        o2i = jnp.einsum('bhwne,nes->bhwns', o1r, w2i) + jnp.einsum('bhwne,nes->bhwns', o1i, w2r) + b2i
        o2r = _softshrink(o2r, LAMBDA)
        o2i = _softshrink(o2i, LAMBDA)
        xc = (o2r + 1j * o2i).reshape(B, H, W // 2 + 1, D)
        out = jnp.fft.irfft2(xc, s=(H, W), axes=(1, 2), norm='ortho')
        return out + residual

    def _gn(v, G=32, eps=1e-5):
        B_, H_, W_, C_ = v.shape
        g = v.reshape(B_, H_, W_, G, C_ // G)
        m = jnp.mean(g, axis=(1, 2, 4), keepdims=True)
        s = jnp.var(g, axis=(1, 2, 4), keepdims=True)
        return ((g - m) / jnp.sqrt(s + eps)).reshape(v.shape)

    def _ln_c(v, eps=1e-6):
        m = jnp.mean(v, axis=-1, keepdims=True)
        s = jnp.var(v, axis=-1, keepdims=True)
        return (v - m) / jnp.sqrt(s + eps)

    def _ln_t(v, eps=1e-5):
        m = jnp.mean(v, axis=-1, keepdims=True)
        s = jnp.var(v, axis=-1, keepdims=True)
        return (v - m) / jnp.sqrt(s + eps)

    def _to_tokens(v):
        B_, H_, W_, C_ = v.shape
        return v.reshape(B_, H_ * W_, C_)
    def _from_tokens(t, like):
        return t.reshape(like.shape)

    x = _L0_conv_ref(x, L0_conv_w1r, L0_conv_w1i, L0_conv_b1r, L0_conv_b1i, L0_conv_w2r, L0_conv_w2i, L0_conv_b2r, L0_conv_b2i)
    return x


_drawn_inputs = setup_inputs


def setup_inputs(seed=0):
    import zlib

    import numpy as np

    out = dict(_drawn_inputs(seed))
    spreads = {'L0_conv_b1r': (0.0, 0.522),
     'L0_conv_b1i': (0.0, 0.521),
     'L0_conv_b2r': (0.0, 0.1),
     'L0_conv_b2i': (0.0, 0.1)}
    factors = {}
    for name, (base, spread) in spreads.items():
        noise = np.random.default_rng([zlib.crc32(name.encode()), seed]).standard_normal(out[name].shape)
        drawn = base * np.exp(spread * noise) if base else spread * noise
        out[name] = jnp.asarray(drawn.astype(out[name].dtype))
    for name, factor in factors.items():
        out[name] = (out[name] * factor).astype(out[name].dtype)
    return out
```

```python
from contextlib import ExitStack

import concourse.bass as bass
import numpy as np
from concourse import mybir
from concourse.alu_op_type import AluOpType as ALU

F32 = mybir.dt.float32
ACT = mybir.ActivationFunctionType

B, H, W, D = 2, 128, 256, 768
NB = 8
C = D // NB
WH = W // 2
K = H // 2 + 1
KM = H - K
NP = WH // 2
T = 2 * NP + 1
UNITS = B * NB
LAMBDA = 0.01
ROWS = 8
GROUPS = H // ROWS
BIAS = 2
SLOTS = 2


def dft_constants():
    h = np.arange(H)[:, None]
    w = np.arange(WH)[:, None]
    k = np.arange(K)[None, :]
    kw = np.concatenate([2 * np.arange(NP) + 1, 2 * np.arange(NP), [WH]])
    angle = 2 * np.pi * ((w * kw[None, :]) % W) / W
    a = np.stack([np.cos(angle), -np.sin(angle)], axis=2) / np.sqrt(W)
    a[:, -1, 1] = 0.0
    a = a.reshape(WH, 2 * T)
    angle = 2 * np.pi * ((h * k) % H) / H
    s, c = np.sin(angle) / np.sqrt(H), np.cos(angle) / np.sqrt(H)
    s[:, K - 1] = 0.0
    hf = np.concatenate([s, c, -s], axis=1)
    kh = np.concatenate([np.arange(K), -np.arange(1, KM + 1)])[:, None]
    angle = 2 * np.pi * ((kh * h.T) % H) / H
    hi = np.concatenate([np.cos(angle), np.sin(angle)], axis=1) / np.sqrt(H)
    wt = np.arange(WH)[None, :]

    def row(kw, im):
        angle = 2 * np.pi * ((kw * wt) % W) / W
        twice = 1.0 if kw in (0, WH) else 2.0
        return (-np.sin(angle) if im else np.cos(angle)) * twice / np.sqrt(W)

    odd = [row(2 * j + 1, im) for j in range(NP) for im in (0, 1)]
    even = [row(0, 0)] + [row(2 * j, im) for j in range(1, NP) for im in (1, 0)] + [row(WH, 0)]
    wi = np.concatenate([np.concatenate(odd), np.concatenate(even)], axis=1)
    every = np.concatenate([a, hf, hi, wi], axis=1)
    return np.ascontiguousarray(every, dtype=np.float32)


A0, HF0 = 0, 2 * T
HI0 = HF0 + 3 * K
WI0 = HI0 + 2 * H
NCONST = WI0 + 2 * WH


def build(nc, x, w1r, w1i, b1r, b1i, w2r, w2i, b2r, b2i, consts, out):
    xv = x.rearrange("b h (j w) (n c) -> b n w h j c", j=2, c=C)
    ov = out.rearrange("b h (j w) (n c) -> b n w h j c", j=2, c=C)

    with ExitStack() as ctx:
        def sb(name, shape):
            return ctx.enter_context(nc.sbuf_tensor(name, shape, F32))

        def sem(name):
            return ctx.enter_context(nc.semaphore(name))

        X = sb("X", [128, H, 2, C])
        YZ = sb("YZ", [128, 2 * T, C])
        const = sb("const", [128, NCONST])
        w1 = sb("w1", [C, 3, C])
        w2 = sb("w2", [C + 1, 3, C])
        b1 = sb("b1", [C, 2])
        work = sb("work", [128, 2312])

        def piece(at, *shape):
            n = int(np.prod(shape))
            v = work[:, at:at + n]
            names = "abc"[:len(shape)]
            return v.rearrange(f"p ({' '.join(names)}) -> p {' '.join(names)}", **dict(zip(names, shape)))

        Xs = piece(0, SLOTS, 2, H)
        o1 = piece(512, SLOTS, 2, H)
        Yr = piece(1024, SLOTS, 2, C)
        PiS = piece(1408, SLOTS, 2 * K)
        res = piece(1928, SLOTS, 2, C)
        A1 = piece(0, SLOTS, 2, H)
        A2 = piece(512, SLOTS, 2, H)
        fold = piece(1024, SLOTS, 2, H)
        G = piece(1536, SLOTS, 2 * H)
        Os = work[:, 2048:2048 + H]

        psum = [ctx.enter_context(nc.psum_tensor(f"ps{i}", [128, 512], F32)) for i in range(8)]
        P = psum[0:2]
        M1 = psum[2:4]
        M2 = psum[4:6]
        PA = psum[6:8]

        Acol = const[:, A0:A0 + 2 * T]
        SCS = const[:, HF0:HF0 + 3 * K]
        HIc = const[:, HI0:HI0 + H]
        HIs = const[:, HI0 + H:HI0 + 2 * H]
        WIo = const[:, WI0:WI0 + WH]
        WIe = const[:, WI0 + WH:WI0 + 2 * WH]

        def view(start, group, step, n):
            return bass.AP(tensor=YZ[:].tensor, offset=start * C,
                           ap=[[2 * T * C, 128], [group * C, 2], [step * C, n], [1, C]])

        Z_rows = view(0, 2 * NP + 1, 1, H)
        Z_im = view(1, 2 * NP - 1, 2, NP)
        Z_re = view(0, 2 * NP + 3, 2, NP)

        counted = {e: {n: sem(n) for n in names} for e, names in {
            "pe": ("h_done", "mix1_done", "mix2_done", "ih_done", "a_done", "iw_done"),
            "act": ("pi_ready", "o1_ready", "g_ready", "y_ready", "odd_ready"),
            "dve": ("xs_ready", "clip_ready", "z_ready", "a12_ready", "out_ready"),
            "pool": ("yr_ready", "fold_ready", "row_added"),
        }.items()}
        (h_done, mix1_done, mix2_done, ih_done, a_done, iw_done) = counted["pe"].values()
        (pi_ready, o1_ready, g_ready, y_ready, odd_ready) = counted["act"].values()
        (xs_ready, clip_ready, z_ready, a12_ready, out_ready) = counted["dve"].values()
        (yr_ready, fold_ready, row_added) = counted["pool"].values()
        weights_ready = sem("weights_ready")
        pool_waits = sem("pool_waits")
        const_in = sem("const_in")
        weights_in = sem("weights_in")
        x_in = sem("x_in")
        res_in = [sem(f"res_in{i}") for i in range(SLOTS)]
        stored = [sem(f"stored{i}") for i in range(SLOTS)]
        WEIGHT_DMAS = 8

        def made(n):
            return n + 1 + BIAS

        def freed(n):
            return n - SLOTS + 1 + BIAS

        block = ctx.enter_context(nc.Block())

        @block.sync
        def _(sp):
            def load_weights(n):
                for dst, src in ((w1[:, 0, :], w1r[n]), (w1[:, 1, :], w1i[n]),
                                 (w2[0:C, 1, :], w2r[n]), (w2[0:C, 2, :], w2i[n]),
                                 (b1[:, 0:1], b1r[n].rearrange("(c a) -> c a", a=1)),
                                 (b1[:, 1:2], b1i[n].rearrange("(c a) -> c a", a=1)),
                                 (w2[C:C + 1, 1, :], b2r[n].rearrange("(a c) -> a c", a=1)),
                                 (w2[C:C + 1, 2, :], b2i[n].rearrange("(a c) -> a c", a=1))):
                    sp.dma_start(dst, src).then_inc(weights_in, 16)

            def load_rows(b, n, g):
                rows = slice(g * ROWS, (g + 1) * ROWS)
                sp.dma_start(X[:, rows], xv[b, n][:, rows]).then_inc(x_in, 16)

            def finish_unit(v, b, n, nxt):
                sp.wait_ge(out_ready, made(C * v + C - 1))
                for g in range(GROUPS + 2):
                    if g < GROUPS:
                        for r in range(ROWS):
                            h = g * ROWS + r
                            if h >= SLOTS:
                                sp.wait_ge(row_added, freed(H * v + h))
                            sp.dma_start(res[:, h % SLOTS], xv[b, n][:, h]).then_inc(res_in[h % SLOTS], 16)
                    if 1 <= g <= GROUPS:
                        rows = slice((g - 1) * ROWS, g * ROWS)
                        sp.wait_ge(row_added, made(H * v + g * ROWS - 1))
                        sp.dma_start(ov[b, n][:, rows], X[:, rows]).then_inc(stored[(g - 1) % SLOTS], 16)
                    if g >= 2 and nxt is not None:
                        sp.wait_ge(stored[g % SLOTS], 16 * (GROUPS // SLOTS * v + (g - 2) // SLOTS + 1))
                        load_rows(*nxt, g - 2)

            def next_weights(u, n):
                sp.wait_ge(mix2_done, made(T * u + T - 1))
                load_weights(n)

            sp.dma_start(const[:], consts).then_inc(const_in, 16)
            for g in range(GROUPS):
                load_rows(0, 0, g)
            load_weights(0)
            sp.wait_ge(fold_ready, made(C - 1))
            for g in range(GROUPS):
                load_rows(1, 0, g)
            next_weights(0, 0)
            with sp.Fori(0, NB - 1) as k:
                finish_unit(2 * k, 0, k, (0, k + 1))
                next_weights(2 * k + 1, k + 1)
                finish_unit(2 * k + 1, 1, k, (1, k + 1))
                next_weights(2 * k + 2, k + 1)
            finish_unit(UNITS - 2, 0, NB - 1, None)
            finish_unit(UNITS - 1, 1, NB - 1, None)
            for s in range(SLOTS):
                sp.wait_ge(stored[s], 16 * (GROUPS // SLOTS) * UNITS)

        @block.tensor
        def _(pe):
            def h_sums(u, t, slot):
                pe.wait_ge(yr_ready, made(T * u + t))
                pe.matmul(P[slot][0:C, 0:2 * K], Yr[:, slot, 0, :], SCS[:, K:3 * K], start=True, stop=True)
                pe.matmul(P[slot][0:C, 2 * K:4 * K], Yr[:, slot, 1, :], SCS[:, 0:2 * K],
                          start=True, stop=True).then_inc(h_done, 1)

            def mix1(u, t, slot):
                pe.wait_ge(xs_ready, made(T * u + t))
                m = M1[slot]
                pe.matmul(m[0:C, 0:H], w1[:, 0, :], Xs[0:C, slot, 0, :], start=True, stop=False)
                pe.matmul(m[0:C, 0:H], w1[:, 2, :], Xs[0:C, slot, 1, :], start=False, stop=True)
                pe.matmul(m[0:C, H:2 * H], w1[:, 1, :], Xs[0:C, slot, 0, :], start=True, stop=False)
                pe.matmul(m[0:C, H:2 * H], w1[:, 0, :], Xs[0:C, slot, 1, :],
                          start=False, stop=True).then_inc(mix1_done, 1)

            def mix2(u, t, slot):
                pe.wait_ge(o1_ready, made(T * u + t))
                m = M2[slot][:, 0:2 * C]
                pe.matmul(m, o1[0:C + 1, slot, 0, :], w2[:, 1:3, :], start=True, stop=False)
                pe.matmul(m, o1[0:C, slot, 1, :], w2[0:C, 0:2, :], start=False, stop=True).then_inc(mix2_done, 1)

            def phase1(u):
                if not (isinstance(u, int) and u == 0):
                    pe.wait_ge(out_ready, made(C * (u - 1) + C - 1))
                h_sums(u, 0, 0)
                h_sums(u, 1, 1)
                pe.wait_ge(weights_ready, u + 1)
                mix1(u, 0, 0)

                def pair(t):
                    for d in range(2):
                        pe.wait_ge(xs_ready, freed(T * u + t + d))
                        h_sums(u, t + d, d)
                        pe.wait_ge(o1_ready, freed(T * u + t + d - 1))
                        mix1(u, t + d - 1, 1 - d)
                        pe.wait_ge(z_ready, freed(T * u + t + d - 2))
                        mix2(u, t + d - 2, d)

                with pe.Fori(1, NP) as i:
                    pair(2 * i)
                pe.wait_ge(xs_ready, freed(T * u + T - 1))
                h_sums(u, T - 1, 0)
                pe.wait_ge(o1_ready, freed(T * u + T - 2))
                mix1(u, T - 2, 1)
                pe.wait_ge(z_ready, freed(T * u + T - 3))
                mix2(u, T - 3, 0)
                pe.wait_ge(o1_ready, freed(T * u + T - 1))
                mix1(u, T - 1, 0)
                pe.wait_ge(z_ready, freed(T * u + T - 2))
                mix2(u, T - 2, 1)
                pe.wait_ge(z_ready, freed(T * u + T - 1))
                mix2(u, T - 1, 0)

            def ih(u, c, slot):
                pe.wait_ge(a12_ready, made(C * u + c))
                pe.wait_ge(g_ready, freed(C * u + c))
                for g in range(2):
                    p = P[slot][:, g * H:(g + 1) * H]
                    pe.matmul(p, A1[:, slot, g, :], HIc, start=True, stop=False)
                    last = pe.matmul(p, A2[:, slot, g, :], HIs, start=False, stop=True)
                last.then_inc(ih_done, 1)

            def a_forward(u, c, slot):
                pe.wait_ge(fold_ready, made(C * u + c))
                pe.wait_ge(y_ready, freed(C * u + c))
                pe.matmul(PA[slot][:, 0:H], fold[:, slot, 0, :], Acol[:, 0:H], start=True, stop=True)
                pe.matmul(PA[slot][:, H:2 * T], fold[:, slot, 1, :], Acol[:, H:2 * T],
                          start=True, stop=True).then_inc(a_done, 1)

            def iw(u, c, slot):
                pe.wait_ge(g_ready, made(C * u + c))
                pe.wait_ge(out_ready, freed(C * u + c))
                pe.matmul(M1[slot][:, 0:H], WIe, G[:, slot, H:2 * H], start=True, stop=True)
                pe.matmul(M1[slot][:, H:2 * H], WIo, G[:, slot, 0:H], start=True, stop=True).then_inc(iw_done, 1)

            def phase2(u, forward):
                def channel(c, slot, first=False):
                    ih(u, c, slot)
                    if forward:
                        a_forward(u + 1, c, slot)
                    if not first:
                        iw(u, c - 1, 1 - slot)

                channel(0, 0, first=True)
                channel(1, 1)
                with pe.Fori(1, C // 2) as i:
                    channel(2 * i, 0)
                    channel(2 * i + 1, 1)
                iw(u, C - 1, 1)

            for s in counted["pe"].values():
                pe.sem_inc(s, BIAS)
            pe.wait_ge(const_in, 16)
            with pe.Fori(0, C // 2) as i:
                a_forward(0, 2 * i, 0)
                a_forward(0, 2 * i + 1, 1)
            phase1(0)
            phase2(0, True)
            with pe.Fori(1, UNITS - 1) as u:
                phase1(u)
                phase2(u, True)
            phase1(UNITS - 1)
            phase2(UNITS - 1, False)

        @block.scalar
        def _(act):
            def copy_pi(u, t, slot):
                act.wait_ge(h_done, made(T * u + t))
                act.activation(PiS[0:C, slot], P[slot][0:C, 2 * K:4 * K], ACT.Copy).then_inc(pi_ready, 1)

            def relu(u, t, slot):
                act.wait_ge(mix1_done, made(T * u + t))
                act.activation(o1[0:C, slot, 0, :], M1[slot][0:C, 0:H], ACT.Relu, bias=b1[:, 0:1])
                act.activation(o1[0:C, slot, 1, :], M1[slot][0:C, H:2 * H], ACT.Relu,
                               bias=b1[:, 1:2]).then_inc(o1_ready, 1)

            def phase1(u):
                copy_pi(u, 0, 0)
                copy_pi(u, 1, 1)
                relu(u, 0, 0)

                def step(t, d, prior=True):
                    act.wait_ge(xs_ready, freed(T * u + t))
                    copy_pi(u, t, d)
                    if prior:
                        act.wait_ge(mix2_done, freed(T * u + t - 1))
                    relu(u, t - 1, 1 - d)

                step(2, 0, prior=False)
                step(3, 1)
                with act.Fori(2, NP) as i:
                    step(2 * i, 0)
                    step(2 * i + 1, 1)
                step(T - 1, 0)
                act.wait_ge(mix2_done, freed(T * u + T - 1))
                relu(u, T - 1, 0)

            def copy_y(u, c, slot):
                act.wait_ge(a_done, made(C * u + c))
                act.activation(YZ[:, :, bass.ds(c, 1)], PA[slot][:, 0:2 * T].rearrange("p (n a) -> p n a", a=1),
                               ACT.Copy).then_inc(y_ready, 1)

            def copy_g(u, c, slot):
                act.wait_ge(ih_done, made(C * u + c))
                act.wait_ge(iw_done, freed(C * u + c))
                act.activation(G[:, slot], P[slot][:, 0:2 * H], ACT.Copy).then_inc(g_ready, 1)

            def copy_odd(u, c, slot):
                act.wait_ge(iw_done, made(C * u + c))
                act.wait_ge(out_ready, made(C * u + c - 1))
                act.activation(Os, M1[slot][:, H:2 * H], ACT.Copy).then_inc(odd_ready, 1)

            def phase2(u, forward):
                act.wait_ge(row_added, H * u + BIAS)

                def channel(c, slot, first=False):
                    copy_g(u, c, slot)
                    if forward:
                        act.wait_ge(a12_ready, made(C * u + c))
                        copy_y(u + 1, c, slot)
                    if not first:
                        copy_odd(u, c - 1, 1 - slot)

                channel(0, 0, first=True)
                channel(1, 1)
                with act.Fori(1, C // 2) as i:
                    channel(2 * i, 0)
                    channel(2 * i + 1, 1)
                copy_odd(u, C - 1, 1)

            for s in counted["act"].values():
                act.sem_inc(s, BIAS)
            with act.Fori(0, C // 2) as i:
                copy_y(0, 2 * i, 0)
                copy_y(0, 2 * i + 1, 1)
            phase1(0)
            phase2(0, True)
            with act.Fori(1, UNITS - 1) as u:
                phase1(u)
                phase2(u, True)
            phase1(UNITS - 1)
            phase2(UNITS - 1, False)

        @block.vector
        def _(dve):
            def combine(u, t, slot):
                dve.wait_ge(pi_ready, made(T * u + t))
                pr, pi, xs = P[slot][0:C, 0:2 * K], PiS[0:C, slot], Xs[0:C, slot]
                dve.tensor_tensor(xs[:, :, 0:K], pr.rearrange("p (a k) -> p a k", a=2),
                                  pi.rearrange("p (a k) -> p a k", a=2), ALU.add)
                dve.tensor_tensor(xs[:, 0, K:H], pr[:, 1:1 + KM], pi[:, 1:1 + KM], ALU.subtract)
                dve.tensor_tensor(xs[:, 1, K:H], pi[:, K + 1:K + 1 + KM], pr[:, K + 1:K + 1 + KM],
                                  ALU.subtract).then_inc(xs_ready, 1)

            def clip(u, t, slot, m, z):
                dve.wait_ge(mix2_done, made(T * u + t))
                dve.tensor_scalar(z, m, LAMBDA, -LAMBDA, ALU.min, ALU.max).then_inc(clip_ready, 1)

            def shrink(u, t, slot, m, z):
                dve.wait_ge(clip_ready, made(T * u + t))
                dve.tensor_tensor(z, m, z, ALU.subtract).then_inc(z_ready, 1)

            def prepare(u):
                dve.wait_ge(weights_in, 16 * WEIGHT_DMAS * (u + 1))
                dve.tensor_scalar(w1[:, 2, :], w1[:, 1, :], -1.0, None, ALU.mult)
                dve.tensor_scalar(w2[0:C, 0, :], w2[0:C, 2, :], -1.0, None, ALU.mult)
                dve.memset(o1[C:C + 1, 0, 0, :], 1.0)
                dve.memset(o1[C:C + 1, 1, 0, :], 1.0).then_inc(weights_ready, 1)

            pairs = YZ[:].rearrange("p (k a) c -> p k a c", a=2)
            z_nyq = pairs[:, 2 * NP]
            mix2_out = [m[:, 0:2 * C].rearrange("p (a c) -> p a c", a=2) for m in M2]
            mix2_out_of = (mix2_out[0], mix2_out[1][:, ::-1])

            def z_of(j, d):
                return pairs[:, bass.ds(d * NP + j, 1)].rearrange("p k a c -> p (k a) c")

            def phase1(u):
                prepare(u)
                combine(u, 0, 0)
                combine(u, 1, 1)

                def step(t, i, d):
                    z = z_of(i - 1, d)
                    clip(u, t - 2, d, mix2_out_of[d], z)
                    dve.wait_ge(mix1_done, freed(T * u + t))
                    combine(u, t, d)
                    shrink(u, t - 2, d, mix2_out_of[d], z)

                with dve.Fori(1, NP) as i:
                    step(2 * i, i, 0)
                    step(2 * i + 1, i, 1)
                step(T - 1, NP, 0)
                z = z_of(NP - 1, 1)
                clip(u, T - 2, 1, mix2_out_of[1], z)
                shrink(u, T - 2, 1, mix2_out_of[1], z)
                m = mix2_out[0]
                clip(u, T - 1, 0, m, z_nyq)
                dve.wait_ge(clip_ready, made(T * u + T - 1))
                dve.tensor_tensor(z_nyq[:, 0], m[:, 0], z_nyq[:, 0], ALU.subtract)
                dve.tensor_tensor(z_nyq[:, 1], z_nyq[:, 1], m[:, 1], ALU.subtract).then_inc(z_ready, 1)

            def gather(u, c, slot):
                def at(v, n):
                    return v[:, :, :, bass.ds(c, 1)].rearrange("p g n a -> p g (n a)")

                dve.tensor_copy(A1[:, slot], at(Z_rows, H))
                a2 = A2[:, slot].rearrange("p g (n a) -> p g n a", a=2)
                dve.tensor_scalar(a2[:, :, :, 0], at(Z_im, NP), -1.0, None, ALU.mult)
                dve.tensor_copy(a2[:, :, :, 1], at(Z_re, NP)).then_inc(a12_ready, 1)

            def write_out(u, c, slot):
                dve.wait_ge(odd_ready, made(C * u + c))
                even = M1[slot][:, 0:H]
                for j, op in ((0, ALU.add), (1, ALU.subtract)):
                    o = X[:, :, j, bass.ds(c, 1)].rearrange("p h a -> p (h a)")
                    last = dve.tensor_tensor(o, even, Os, op)
                last.then_inc(out_ready, 1)

            def phase2(u, forward):
                dve.wait_ge(z_ready, made(T * u + T - 1))
                if not forward:
                    for s in stored:
                        dve.wait_ge(s, 16 * (GROUPS // SLOTS) * u)
                gather(u, 0, 0)
                gather(u, 1, 1)

                def channel(c, slot):
                    dve.wait_ge(ih_done, freed(C * u + c))
                    gather(u, c, slot)
                    if forward:
                        dve.wait_ge(fold_ready, made(C * (u + 1) + c - 2))
                    write_out(u, c - 2, slot)

                with dve.Fori(1, C // 2) as i:
                    channel(2 * i, 0)
                    channel(2 * i + 1, 1)
                for c in (C - 2, C - 1):
                    if forward:
                        dve.wait_ge(fold_ready, made(C * (u + 1) + c))
                    write_out(u, c, c % 2)

            for s in counted["dve"].values():
                dve.sem_inc(s, BIAS)
            phase1(0)
            phase2(0, True)
            with dve.Fori(1, UNITS - 1) as u:
                phase1(u)
                phase2(u, True)
            phase1(UNITS - 1)
            phase2(UNITS - 1, False)

        @block.gpsimd
        def _(pool):
            Y = YZ[:].rearrange("p (k a) c -> p k a c", a=2)

            def copy_yr(u, t, slot, k):
                pool.tensor_copy(Yr[:, slot], Y[:, bass.ds(k, 1)].rearrange("p k a c -> p (k a) c")
                                 ).then_inc(yr_ready, 1)

            def alone():
                pool.sem_inc(pool_waits, 1)

            def phase1(u, residual):
                pool.wait_ge(y_ready, made(C * u + C - 1))
                alone()
                copy_yr(u, 0, 0, 0)
                copy_yr(u, 1, 1, NP)
                if residual:
                    add_pair(u - 1, 0)
                with pool.Fori(1, NP) as i:
                    for d in range(2):
                        pool.wait_ge(h_done, freed(T * u + 2 * i + d))
                        copy_yr(u, 2 * i + d, d, i + d * NP)
                    if residual:
                        add_pair(u - 1, i)
                pool.wait_ge(h_done, freed(T * u + T - 1))
                alone()
                copy_yr(u, T - 1, 0, 2 * NP)

            def add_pair(v, i):
                for d in range(2):
                    pool.wait_ge(res_in[d], 16 * (NP * v + i + 1))
                    row = X[:, bass.ds(2 * i + d, 1)].rearrange("p h j c -> p (h j) c")
                    pool.tensor_tensor(row, row, res[:, d], ALU.add).then_inc(row_added, 1)

            def fold_channel(u, c, slot):
                pool.wait_ge(a_done, freed(C * u + c))
                lo, hi = (X[:, :, j, bass.ds(c, 1)].rearrange("p h a -> p (h a)") for j in (0, 1))
                pool.tensor_tensor(fold[:, slot, 0, :], lo, hi, ALU.subtract)
                pool.tensor_tensor(fold[:, slot, 1, :], lo, hi, ALU.add).then_inc(fold_ready, 1)

            def fold_unit(u):
                pool.wait_ge(x_in, 16 * GROUPS * (u + 1))
                alone()
                with pool.Fori(0, C // 2) as i:
                    fold_channel(u, 2 * i, 0)
                    fold_channel(u, 2 * i + 1, 1)

            for s in counted["pool"].values():
                pool.sem_inc(s, BIAS)
            fold_unit(0)
            phase1(0, residual=False)
            pool.wait_ge(xs_ready, made(T - 1))
            fold_unit(1)
            with pool.Fori(1, UNITS - 1) as u:
                phase1(u, residual=True)
                pool.wait_ge(xs_ready, made(T * u + T - 1))
                fold_unit(u + 1)
            phase1(UNITS - 1, residual=True)
            with pool.Fori(0, NP) as i:
                add_pair(UNITS - 1, i)


def kernel(x, L0_conv_w1r, L0_conv_w1i, L0_conv_b1r, L0_conv_b1i,
           L0_conv_w2r, L0_conv_w2i, L0_conv_b2r, L0_conv_b2i):
    import concourse.bacc as bacc
    from concourse.bass_utils import run_bass_kernel_spmd

    nc = bacc.Bacc("TRN2", target_bir_lowering=False, num_devices=1)
    arrays = {
        "x": x, "w1r": L0_conv_w1r, "w1i": L0_conv_w1i, "b1r": L0_conv_b1r, "b1i": L0_conv_b1i,
        "w2r": L0_conv_w2r, "w2i": L0_conv_w2i, "b2r": L0_conv_b2r, "b2i": L0_conv_b2i,
        "consts": dft_constants(),
    }
    arrays = {f"in_{k}": np.ascontiguousarray(v) for k, v in arrays.items()}
    args = [nc.dram_tensor(k, v.shape, F32, kind="ExternalInput").ap() for k, v in arrays.items()]
    out = nc.dram_tensor("out", (B, H, W, D), F32, kind="ExternalOutput").ap()
    build(nc, *args, out)
    r = run_bass_kernel_spmd(nc, [arrays], core_ids=[0])
    return r.results[0]["out"]
```

```python
from contextlib import ExitStack

import concourse.bass as bass
import numpy as np
from concourse import mybir
from concourse.alu_op_type import AluOpType as ALU

F32 = mybir.dt.float32
ACT = mybir.ActivationFunctionType

B, H, W, D = 2, 128, 256, 768
NB = 8
C = D // NB
WH = W // 2
K = H // 2 + 1
KM = H - K
NP = WH // 2
T = 2 * NP + 1
UNITS = B * NB
LAMBDA = 0.01
GROUPS = 8
LAG = 4
BIAS = 2
SLOTS = 2


def dft_constants():
    h = np.arange(H)[:, None]
    w = np.arange(WH)[:, None]
    k = np.arange(K)[None, :]
    kw = np.concatenate([2 * np.arange(NP) + 1, 2 * np.arange(NP), [WH]])
    angle = 2 * np.pi * ((w * kw[None, :]) % W) / W
    a = np.stack([np.cos(angle), -np.sin(angle)], axis=2) / np.sqrt(W)
    a[:, -1, 1] = 0.0
    a = a.reshape(WH, 2 * T)
    angle = 2 * np.pi * ((h * k) % H) / H
    s, c = np.sin(angle) / np.sqrt(H), np.cos(angle) / np.sqrt(H)
    s[:, K - 1] = 0.0
    hf = np.concatenate([s, c, -s], axis=1)
    kh = np.concatenate([np.arange(K), -np.arange(1, KM + 1)])[:, None]
    angle = 2 * np.pi * ((kh * h.T) % H) / H
    hi = np.concatenate([np.cos(angle), np.sin(angle)], axis=1) / np.sqrt(H)
    wt = np.arange(WH)[None, :]

    def row(kw, im):
        angle = 2 * np.pi * ((kw * wt) % W) / W
        twice = 1.0 if kw in (0, WH) else 2.0
        return (-np.sin(angle) if im else np.cos(angle)) * twice / np.sqrt(W)

    odd = [row(2 * j + 1, im) for j in range(NP) for im in (0, 1)]
    even = [row(0, 0)] + [row(2 * j, im) for j in range(1, NP) for im in (1, 0)] + [row(WH, 0)]
    wi = np.concatenate([np.concatenate(odd), np.concatenate(even)], axis=1)
    every = np.concatenate([a, hf, hi, wi], axis=1)
    return np.ascontiguousarray(every, dtype=np.float32)


A0, HF0 = 0, 2 * T
HI0 = HF0 + 3 * K
WI0 = HI0 + 2 * H
NCONST = WI0 + 2 * WH


def build(nc, x, w1r, w1i, b1r, b1i, w2r, w2i, b2r, b2i, consts, out):
    xv = x.rearrange("b h (j w) (n c) -> b n w h j c", j=2, c=C)
    ov = out.rearrange("b h (j w) (n c) -> b n w h j c", j=2, c=C)

    with ExitStack() as ctx:
        def sb(name, shape):
            return ctx.enter_context(nc.sbuf_tensor(name, shape, F32))

        def sem(name):
            return ctx.enter_context(nc.semaphore(name))

        X = sb("X", [128, H, 2, C])
        YZ = sb("YZ", [128, 2 * T, C])
        const = sb("const", [128, NCONST])
        w1 = sb("w1", [C, 3, C])
        w2 = sb("w2", [C + 1, 3, C])
        b1 = sb("b1", [C, 2])
        work = sb("work", [128, 2312])

        def piece(at, *shape):
            n = int(np.prod(shape))
            v = work[:, at:at + n]
            names = "abc"[:len(shape)]
            return v.rearrange(f"p ({' '.join(names)}) -> p {' '.join(names)}", **dict(zip(names, shape)))

        Xs = piece(0, SLOTS, 2, H)
        o1 = piece(512, SLOTS, 2, H)
        Yr = piece(1024, SLOTS, 2, C)
        PiS = piece(1408, SLOTS, 2 * K)
        res = piece(1928, SLOTS, 2, C)
        A1 = piece(0, SLOTS, 2, H)
        A2 = piece(512, SLOTS, 2, H)
        fold = piece(1024, SLOTS, 2, H)
        G = piece(1536, SLOTS, 2 * H)
        Os = piece(2048, SLOTS, H)

        psum = [ctx.enter_context(nc.psum_tensor(f"ps{i}", [128, 512], F32)) for i in range(8)]
        P = psum[0:2]
        M1 = psum[2:4]
        M2 = psum[4:6]
        PA = psum[6:8]

        Acol = const[:, A0:A0 + 2 * T]
        SCS = const[:, HF0:HF0 + 3 * K]
        HIc = const[:, HI0:HI0 + H]
        HIs = const[:, HI0 + H:HI0 + 2 * H]
        WIo = const[:, WI0:WI0 + WH]
        WIe = const[:, WI0 + WH:WI0 + 2 * WH]

        def view(start, group, step, n):
            return bass.AP(tensor=YZ[:].tensor, offset=start * C,
                           ap=[[2 * T * C, 128], [group * C, 2], [step * C, n], [1, C]])

        Z_rows = view(0, 2 * NP + 1, 1, H)
        Z_im = view(1, 2 * NP - 1, 2, NP)
        Z_re = view(0, 2 * NP + 3, 2, NP)

        counted = {e: {n: sem(n) for n in names} for e, names in {
            "pe": ("h_done", "mix1_done", "mix2_done", "ih_done", "a_done", "iw_done"),
            "act": ("yr_ready", "pi_ready", "o1_ready", "g_ready", "y_ready", "odd_ready"),
            "dve": ("xs_ready", "clip_ready", "z_ready", "a12_ready", "out_ready"),
            "pool": ("fold_ready", "row_added", "last_added"),
        }.items()}
        (h_done, mix1_done, mix2_done, ih_done, a_done, iw_done) = counted["pe"].values()
        (yr_ready, pi_ready, o1_ready, g_ready, y_ready, odd_ready) = counted["act"].values()
        (xs_ready, clip_ready, z_ready, a12_ready, out_ready) = counted["dve"].values()
        (fold_ready, row_added, last_added) = counted["pool"].values()
        weights_ready = sem("weights_ready")
        pool_waits = sem("pool_waits")
        const_in = sem("const_in")
        weights_in = sem("weights_in")
        x_in = sem("x_in")
        res_in = [sem(f"res_in{i}") for i in range(SLOTS)]
        stored = [sem(f"stored{i}") for i in range(LAG)]
        WEIGHT_DMAS = 8

        def made(n):
            return n + 1 + BIAS

        def freed(n):
            return n - SLOTS + 1 + BIAS

        def x_loads(u):
            return 16 * (2 * GROUPS + H // 2 * (u - 1))

        block = ctx.enter_context(nc.Block())

        @block.sync
        def _(sp):
            def load_weights(n):
                for dst, src in ((w1[:, 0, :], w1r[n]), (w1[:, 1, :], w1i[n]),
                                 (w2[0:C, 1, :], w2r[n]), (w2[0:C, 2, :], w2i[n]),
                                 (b1[:, 0:1], b1r[n].rearrange("(c a) -> c a", a=1)),
                                 (b1[:, 1:2], b1i[n].rearrange("(c a) -> c a", a=1)),
                                 (w2[C:C + 1, 1, :], b2r[n].rearrange("(a c) -> a c", a=1)),
                                 (w2[C:C + 1, 2, :], b2i[n].rearrange("(a c) -> a c", a=1))):
                    sp.dma_start(dst, src).then_inc(weights_in, 16)

            def load_unit(b, n):
                for g in range(GROUPS):
                    rows = slice(g * H // GROUPS, (g + 1) * H // GROUPS)
                    sp.dma_start(X[:, rows], xv[b, n][:, rows]).then_inc(x_in, 16)

            def finish_unit(v, b, n, nxt):
                def turn(i, d, load=True, store=True, replace=True):
                    p = LAG * i + d
                    if load:
                        for r in range(SLOTS):
                            sp.wait_ge(row_added, freed(H * v + 2 * p + r))
                            sp.dma_start(res[:, r], xv[b, n][:, bass.ds(2 * p + r, 1)].rearrange(
                                "w h j c -> w (h j) c")).then_inc(res_in[r], 16)
                    if store:
                        sp.wait_ge(row_added, made(H * v + 2 * p - 1))
                        rows = bass.ds(2 * p - 2, 2)
                        sp.dma_start(ov[b, n][:, rows], X[:, rows]).then_inc(stored[(d - 1) % LAG], 16)
                    if replace:
                        sp.wait_ge(stored[d], 16 * (H // 2 // LAG * v + i))
                        rows = bass.ds(2 * p - 2 * LAG, 2)
                        sp.dma_start(X[:, rows], xv[nxt[0], nxt[1]][:, rows]).then_inc(x_in, 16)

                sp.wait_ge(out_ready, made(C * v + C - 1))
                for d in range(LAG):
                    turn(0, d, store=d > 0, replace=False)
                with sp.Fori(1, H // 2 // LAG) as i:
                    for d in range(LAG):
                        turn(i, d)
                for d in range(LAG):
                    turn(H // 2 // LAG, d, load=False, store=d == 0)

            def next_weights(u, n):
                sp.wait_ge(mix2_done, made(T * u + T - 1))
                load_weights(n)

            sp.dma_start(const[:], consts).then_inc(const_in, 16)
            load_unit(0, 0)
            load_weights(0)
            sp.wait_ge(fold_ready, made(C - 1))
            load_unit(1, 0)
            next_weights(0, 0)
            with sp.Fori(0, NB - 1) as k:
                finish_unit(2 * k, 0, k, (0, k + 1))
                next_weights(2 * k + 1, k + 1)
                finish_unit(2 * k + 1, 1, k, (1, k + 1))
                next_weights(2 * k + 2, k + 1)
            finish_unit(UNITS - 2, 0, NB - 1, (1, NB - 1))
            sp.wait_ge(last_added, made(C - 1))
            for g in range(GROUPS):
                rows = slice(g * H // GROUPS, (g + 1) * H // GROUPS)
                sp.dma_start(ov[1, NB - 1][:, rows], X[:, rows]).then_inc(stored[g % LAG], 16)
            for s in range(LAG):
                sp.wait_ge(stored[s], 16 * (H // 2 // LAG * (UNITS - 1) + GROUPS // LAG))

        @block.tensor
        def _(pe):
            def h_sums(u, t, slot):
                pe.wait_ge(yr_ready, made(T * u + t))
                pe.matmul(P[slot][0:C, 0:2 * K], Yr[:, slot, 0, :], SCS[:, K:3 * K], start=True, stop=True)
                pe.matmul(P[slot][0:C, 2 * K:4 * K], Yr[:, slot, 1, :], SCS[:, 0:2 * K],
                          start=True, stop=True).then_inc(h_done, 1)

            def mix1(u, t, slot):
                pe.wait_ge(xs_ready, made(T * u + t))
                m = M1[slot]
                pe.matmul(m[0:C, 0:H], w1[:, 0, :], Xs[0:C, slot, 0, :], start=True, stop=False)
                pe.matmul(m[0:C, 0:H], w1[:, 2, :], Xs[0:C, slot, 1, :], start=False, stop=True)
                pe.matmul(m[0:C, H:2 * H], w1[:, 1, :], Xs[0:C, slot, 0, :], start=True, stop=False)
                pe.matmul(m[0:C, H:2 * H], w1[:, 0, :], Xs[0:C, slot, 1, :],
                          start=False, stop=True).then_inc(mix1_done, 1)

            def mix2(u, t, slot):
                pe.wait_ge(o1_ready, made(T * u + t))
                m = M2[slot][:, 0:2 * C]
                pe.matmul(m, o1[0:C + 1, slot, 0, :], w2[:, 1:3, :], start=True, stop=False)
                pe.matmul(m, o1[0:C, slot, 1, :], w2[0:C, 0:2, :], start=False, stop=True).then_inc(mix2_done, 1)

            def phase1(u):
                if not (isinstance(u, int) and u == 0):
                    pe.wait_ge(out_ready, made(C * (u - 1) + C - 1))
                h_sums(u, 0, 0)
                h_sums(u, 1, 1)
                pe.wait_ge(weights_ready, u + 1)
                mix1(u, 0, 0)

                def pair(t):
                    for d in range(2):
                        pe.wait_ge(xs_ready, freed(T * u + t + d))
                        h_sums(u, t + d, d)
                        pe.wait_ge(o1_ready, freed(T * u + t + d - 1))
                        mix1(u, t + d - 1, 1 - d)
                        pe.wait_ge(z_ready, freed(T * u + t + d - 2))
                        mix2(u, t + d - 2, d)

                with pe.Fori(0, (NP - 1) // 3) as i:
                    for d in range(3):
                        pair(6 * i + 2 * d + 2)
                pe.wait_ge(xs_ready, freed(T * u + T - 1))
                h_sums(u, T - 1, 0)
                pe.wait_ge(o1_ready, freed(T * u + T - 2))
                mix1(u, T - 2, 1)
                pe.wait_ge(z_ready, freed(T * u + T - 3))
                mix2(u, T - 3, 0)
                pe.wait_ge(o1_ready, freed(T * u + T - 1))
                mix1(u, T - 1, 0)
                pe.wait_ge(z_ready, freed(T * u + T - 2))
                mix2(u, T - 2, 1)
                pe.wait_ge(z_ready, freed(T * u + T - 1))
                mix2(u, T - 1, 0)

            def ih(u, c, slot):
                pe.wait_ge(a12_ready, made(C * u + c))
                pe.wait_ge(g_ready, freed(C * u + c))
                for g in range(2):
                    p = P[slot][:, g * H:(g + 1) * H]
                    pe.matmul(p, A1[:, slot, g, :], HIc, start=True, stop=False)
                    last = pe.matmul(p, A2[:, slot, g, :], HIs, start=False, stop=True)
                last.then_inc(ih_done, 1)

            def a_forward(u, c, slot):
                pe.wait_ge(fold_ready, made(C * u + c))
                pe.wait_ge(y_ready, freed(C * u + c))
                pe.matmul(PA[slot][:, 0:H], fold[:, slot, 0, :], Acol[:, 0:H], start=True, stop=True)
                pe.matmul(PA[slot][:, H:2 * T], fold[:, slot, 1, :], Acol[:, H:2 * T],
                          start=True, stop=True).then_inc(a_done, 1)

            def iw(u, c, slot):
                pe.wait_ge(g_ready, made(C * u + c))
                pe.wait_ge(out_ready, freed(C * u + c))
                pe.matmul(M1[slot][:, 0:H], WIe, G[:, slot, H:2 * H], start=True, stop=True)
                pe.matmul(M1[slot][:, H:2 * H], WIo, G[:, slot, 0:H], start=True, stop=True).then_inc(iw_done, 1)

            def phase2(u, forward):
                def channel(c, slot, first=False):
                    ih(u, c, slot)
                    if forward:
                        a_forward(u + 1, c, slot)
                    if not first:
                        iw(u, c - 1, 1 - slot)

                channel(0, 0, first=True)
                channel(1, 1)
                for c in range(2, 6):
                    channel(c, c % 2)
                with pe.Fori(1, C // 6) as i:
                    for d in range(6):
                        channel(6 * i + d, d % 2)
                iw(u, C - 1, 1)

            for s in counted["pe"].values():
                pe.sem_inc(s, BIAS)
            pe.wait_ge(const_in, 16)
            with pe.Fori(0, C // 4) as i:
                for d in range(4):
                    a_forward(0, 4 * i + d, d % 2)
            phase1(0)
            phase2(0, True)
            with pe.Fori(1, UNITS - 1) as u:
                phase1(u)
                phase2(u, True)
            phase1(UNITS - 1)
            phase2(UNITS - 1, False)

        @block.scalar
        def _(act):
            Y = YZ[:].rearrange("p (k a) c -> p k a c", a=2)

            def copy_pi(u, t, slot):
                act.wait_ge(h_done, made(T * u + t))
                act.activation(PiS[0:C, slot], P[slot][0:C, 2 * K:4 * K], ACT.Copy).then_inc(pi_ready, 1)

            def relu(u, t, slot):
                act.wait_ge(mix1_done, made(T * u + t))
                act.activation(o1[0:C, slot, 0, :], M1[slot][0:C, 0:H], ACT.Relu, bias=b1[:, 0:1])
                act.activation(o1[0:C, slot, 1, :], M1[slot][0:C, H:2 * H], ACT.Relu,
                               bias=b1[:, 1:2]).then_inc(o1_ready, 1)

            def copy_yr(u, t, slot, k):
                act.activation(Yr[:, slot], Y[:, bass.ds(k, 1)].rearrange("p k a c -> p (k a) c"),
                               ACT.Copy).then_inc(yr_ready, 1)

            def phase1(u):
                act.wait_ge(y_ready, made(C * u + C - 1))
                copy_yr(u, 0, 0, 0)
                copy_yr(u, 1, 1, NP)
                copy_pi(u, 0, 0)

                def step(t, d, k):
                    if k is not None:
                        act.wait_ge(h_done, freed(T * u + t + 1))
                        copy_yr(u, t + 1, 1 - d, k)
                    act.wait_ge(xs_ready, freed(T * u + t))
                    copy_pi(u, t, d)
                    act.wait_ge(mix2_done, freed(T * u + t - 1))
                    relu(u, t - 1, 1 - d)

                step(1, 1, 1)
                with act.Fori(0, (NP - 2) // 2) as j:
                    for i in (2 * j + 1, 2 * j + 2):
                        step(2 * i, 0, NP + i)
                        step(2 * i + 1, 1, i + 1)
                step(T - 3, 0, 2 * NP - 1)
                step(T - 2, 1, 2 * NP)
                step(T - 1, 0, None)
                act.wait_ge(mix2_done, freed(T * u + T - 1))
                relu(u, T - 1, 0)

            def copy_y(u, c, slot):
                act.wait_ge(a_done, made(C * u + c))
                act.activation(YZ[:, :, bass.ds(c, 1)], PA[slot][:, 0:2 * T].rearrange("p (n a) -> p n a", a=1),
                               ACT.Copy).then_inc(y_ready, 1)

            def copy_g(u, c, slot):
                act.wait_ge(ih_done, made(C * u + c))
                act.wait_ge(iw_done, freed(C * u + c))
                act.activation(G[:, slot], P[slot][:, 0:2 * H], ACT.Copy).then_inc(g_ready, 1)

            def copy_odd(u, c, slot):
                act.wait_ge(iw_done, made(C * u + c))
                act.wait_ge(out_ready, freed(C * u + c))
                act.activation(Os[:, slot], M1[slot][:, H:2 * H], ACT.Copy).then_inc(odd_ready, 1)

            def phase2(u, forward):
                act.wait_ge(row_added, H * u + BIAS)

                def channel(c, slot, first=False):
                    copy_g(u, c, slot)
                    if forward:
                        act.wait_ge(a12_ready, made(C * u + c))
                        copy_y(u + 1, c, slot)
                    if not first:
                        copy_odd(u, c - 1, 1 - slot)

                channel(0, 0, first=True)
                channel(1, 1)
                for c in range(2, 6):
                    channel(c, c % 2)
                with act.Fori(1, C // 6) as i:
                    for d in range(6):
                        channel(6 * i + d, d % 2)
                copy_odd(u, C - 1, 1)

            for s in counted["act"].values():
                act.sem_inc(s, BIAS)
            copy_y(0, 0, 0)
            copy_y(0, 1, 1)
            with act.Fori(1, C // 2) as i:
                copy_y(0, 2 * i, 0)
                copy_y(0, 2 * i + 1, 1)
            phase1(0)
            phase2(0, True)
            with act.Fori(1, UNITS - 1) as u:
                phase1(u)
                phase2(u, True)
            phase1(UNITS - 1)
            phase2(UNITS - 1, False)

        @block.vector
        def _(dve):
            def combine(u, t, slot):
                dve.wait_ge(pi_ready, made(T * u + t))
                pr, pi, xs = P[slot][0:C, 0:2 * K], PiS[0:C, slot], Xs[0:C, slot]
                dve.tensor_tensor(xs[:, :, 0:K], pr.rearrange("p (a k) -> p a k", a=2),
                                  pi.rearrange("p (a k) -> p a k", a=2), ALU.add)
                dve.tensor_tensor(xs[:, 0, K:H], pr[:, 1:1 + KM], pi[:, 1:1 + KM], ALU.subtract)
                dve.tensor_tensor(xs[:, 1, K:H], pi[:, K + 1:K + 1 + KM], pr[:, K + 1:K + 1 + KM],
                                  ALU.subtract).then_inc(xs_ready, 1)

            def clip(u, t, slot, m, z):
                dve.wait_ge(mix2_done, made(T * u + t))
                dve.tensor_scalar(z, m, LAMBDA, -LAMBDA, ALU.min, ALU.max).then_inc(clip_ready, 1)

            def shrink(u, t, slot, m, z):
                dve.wait_ge(clip_ready, made(T * u + t))
                dve.tensor_tensor(z, m, z, ALU.subtract).then_inc(z_ready, 1)

            def prepare(u):
                dve.wait_ge(weights_in, 16 * WEIGHT_DMAS * (u + 1))
                dve.tensor_scalar(w1[:, 2, :], w1[:, 1, :], -1.0, None, ALU.mult)
                dve.tensor_scalar(w2[0:C, 0, :], w2[0:C, 2, :], -1.0, None, ALU.mult)
                dve.memset(o1[C:C + 1, 0, 0, :], 1.0)
                dve.memset(o1[C:C + 1, 1, 0, :], 1.0).then_inc(weights_ready, 1)

            pairs = YZ[:].rearrange("p (k a) c -> p k a c", a=2)
            z_nyq = pairs[:, 2 * NP]
            mix2_out = [m[:, 0:2 * C].rearrange("p (a c) -> p a c", a=2) for m in M2]
            mix2_out_of = (mix2_out[0], mix2_out[1][:, ::-1])

            def z_of(j, d):
                return pairs[:, bass.ds(d * NP + j, 1)].rearrange("p k a c -> p (k a) c")

            def phase1(u):
                prepare(u)
                combine(u, 0, 0)
                combine(u, 1, 1)

                def step(t, i, d):
                    z = z_of(i - 1, d)
                    dve.wait_ge(mix1_done, freed(T * u + t))
                    combine(u, t, d)
                    clip(u, t - 2, d, mix2_out_of[d], z)
                    shrink(u, t - 2, d, mix2_out_of[d], z)

                with dve.Fori(0, (NP - 1) // 3) as j:
                    for d in range(3):
                        step(6 * j + 2 * d + 2, 3 * j + d + 1, 0)
                        step(6 * j + 2 * d + 3, 3 * j + d + 1, 1)
                step(T - 1, NP, 0)
                z = z_of(NP - 1, 1)
                clip(u, T - 2, 1, mix2_out_of[1], z)
                shrink(u, T - 2, 1, mix2_out_of[1], z)
                m = mix2_out[0]
                clip(u, T - 1, 0, m, z_nyq)
                dve.wait_ge(clip_ready, made(T * u + T - 1))
                dve.tensor_tensor(z_nyq[:, 0], m[:, 0], z_nyq[:, 0], ALU.subtract)
                dve.tensor_tensor(z_nyq[:, 1], z_nyq[:, 1], m[:, 1], ALU.subtract).then_inc(z_ready, 1)

            def gather(u, c, slot):
                def at(v, n):
                    return v[:, :, :, bass.ds(c, 1)].rearrange("p g n a -> p g (n a)")

                dve.tensor_copy(A1[:, slot], at(Z_rows, H))
                a2 = A2[:, slot].rearrange("p g (n a) -> p g n a", a=2)
                dve.tensor_scalar(a2[:, :, :, 0], at(Z_im, NP), -1.0, None, ALU.mult)
                dve.tensor_copy(a2[:, :, :, 1], at(Z_re, NP)).then_inc(a12_ready, 1)

            def write_out(u, c, slot, forward):
                if forward:
                    dve.wait_ge(fold_ready, made(C * (u + 1) + c))
                    place = [X[:, :, j, bass.ds(c, 1)].rearrange("p h a -> p (h a)") for j in (0, 1)]
                else:
                    dve.wait_ge(last_added, freed(c))
                    place = [fold[:, slot, j, :] for j in (0, 1)]
                dve.wait_ge(odd_ready, made(C * u + c))
                even = M1[slot][:, 0:H]
                dve.tensor_tensor(place[0], even, Os[:, slot], ALU.add)
                dve.tensor_tensor(place[1], even, Os[:, slot], ALU.subtract).then_inc(out_ready, 1)

            def phase2(u, forward):
                dve.wait_ge(z_ready, made(T * u + T - 1))
                gather(u, 0, 0)
                gather(u, 1, 1)

                def channel(c, slot):
                    dve.wait_ge(ih_done, freed(C * u + c))
                    gather(u, c, slot)
                    if not (isinstance(c, int) and c < 3):
                        write_out(u, c - 3, 1 - slot, forward)

                for c in range(2, 6):
                    channel(c, c % 2)
                with dve.Fori(1, C // 6) as i:
                    for d in range(6):
                        channel(6 * i + d, d % 2)
                for c in (C - 3, C - 2, C - 1):
                    write_out(u, c, c % 2, forward)

            def fold_first(c, slot):
                dve.wait_ge(a_done, freed(c))
                lo, hi = (X[:, :, j, bass.ds(c, 1)].rearrange("p h a -> p (h a)") for j in (0, 1))
                dve.tensor_tensor(fold[:, slot, 0, :], lo, hi, ALU.subtract)
                dve.tensor_tensor(fold[:, slot, 1, :], lo, hi, ALU.add).then_inc(fold_ready, 1)

            for s in counted["dve"].values():
                dve.sem_inc(s, BIAS)
            dve.wait_ge(x_in, 16 * GROUPS)
            with dve.Fori(0, C // 4) as i:
                for d in range(4):
                    fold_first(4 * i + d, d % 2)
            phase1(0)
            phase2(0, True)
            with dve.Fori(1, UNITS - 1) as u:
                phase1(u)
                phase2(u, True)
            phase1(UNITS - 1)
            phase2(UNITS - 1, False)

        @block.gpsimd
        def _(pool):
            def alone():
                pool.sem_inc(pool_waits, 1)

            def add_rows(v, i):
                for d in range(2):
                    pool.wait_ge(res_in[d], 16 * (NP * v + i + 1))
                    row = X[:, bass.ds(2 * i + d, 1)].rearrange("p h j c -> p (h j) c")
                    pool.tensor_tensor(row, row, res[:, d], ALU.add).then_inc(row_added, 1)

            def add_unit(v):
                with pool.Fori(0, NP // 2) as i:
                    add_rows(v, 2 * i)
                    add_rows(v, 2 * i + 1)

            def fold_channel(u, c, slot):
                pool.wait_ge(a_done, freed(C * u + c))
                lo, hi = (X[:, :, j, bass.ds(c, 1)].rearrange("p h a -> p (h a)") for j in (0, 1))
                pool.tensor_tensor(fold[:, slot, 0, :], lo, hi, ALU.subtract)
                pool.tensor_tensor(fold[:, slot, 1, :], lo, hi, ALU.add).then_inc(fold_ready, 1)

            def fold_unit(u):
                pool.wait_ge(xs_ready, made(T * (u - 1) + T - 1))
                alone()
                pool.wait_ge(x_in, x_loads(u))
                alone()
                with pool.Fori(0, C // 4) as i:
                    for d in range(4):
                        fold_channel(u, 4 * i + d, d % 2)

            def add_last(c, slot):
                pool.wait_ge(out_ready, made(C * (UNITS - 1) + c))
                for j in range(2):
                    xc = X[:, :, j, bass.ds(c, 1)].rearrange("p h a -> p (h a)")
                    last = pool.tensor_tensor(xc, xc, fold[:, slot, j, :], ALU.add)
                last.then_inc(last_added, 1)

            for s in counted["pool"].values():
                pool.sem_inc(s, BIAS)
            fold_unit(1)
            with pool.Fori(1, UNITS - 1) as u:
                add_unit(u - 1)
                fold_unit(u + 1)
            add_unit(UNITS - 2)
            pool.wait_ge(x_in, x_loads(UNITS))
            with pool.Fori(0, C // 4) as i:
                for d in range(4):
                    add_last(4 * i + d, d % 2)


def kernel(x, L0_conv_w1r, L0_conv_w1i, L0_conv_b1r, L0_conv_b1i,
           L0_conv_w2r, L0_conv_w2i, L0_conv_b2r, L0_conv_b2i):
    import concourse.bacc as bacc
    from concourse.bass_utils import run_bass_kernel_spmd

    nc = bacc.Bacc("TRN2", target_bir_lowering=False, num_devices=1)
    arrays = {
        "x": x, "w1r": L0_conv_w1r, "w1i": L0_conv_w1i, "b1r": L0_conv_b1r, "b1i": L0_conv_b1i,
        "w2r": L0_conv_w2r, "w2i": L0_conv_w2i, "b2r": L0_conv_b2r, "b2i": L0_conv_b2i,
        "consts": dft_constants(),
    }
    arrays = {f"in_{k}": np.ascontiguousarray(v) for k, v in arrays.items()}
    args = [nc.dram_tensor(k, v.shape, F32, kind="ExternalInput").ap() for k, v in arrays.items()]
    out = nc.dram_tensor("out", (B, H, W, D), F32, kind="ExternalOutput").ap()
    build(nc, *args, out)
    r = run_bass_kernel_spmd(nc, [arrays], core_ids=[0])
    return r.results[0]["out"]
```

```python
from contextlib import ExitStack

import concourse.bass as bass
import numpy as np
from concourse import mybir
from concourse.alu_op_type import AluOpType as ALU

F32 = mybir.dt.float32
ACT = mybir.ActivationFunctionType

B, H, W, D = 2, 128, 256, 768
NB = 8
C = D // NB
PAIRS = C // 2
WH = W // 2
K = H // 2 + 1
KM = H - K
NP = WH // 2
KW = 2 * NP + 1
T = KW + 2
UNITS = B * NB
LAMBDA = 0.01
GROUPS = 8
MIRRORED = (1, 3)
LAG = 4
SLOTS = 2
BIAS = SLOTS
DEEP = 4


def dft_constants():
    w = np.arange(WH)[:, None]
    kw = np.concatenate([2 * np.arange(NP) + 1, 2 * np.arange(NP), [WH]])
    angle = 2 * np.pi * ((w * kw[None, :]) % W) / W
    a = np.stack([np.cos(angle), -np.sin(angle)], axis=2) / np.sqrt(W)
    a = a.reshape(WH, 2 * KW)
    angle = 2 * np.pi * ((np.arange(H)[:, None] * np.arange(K)[None, :]) % H) / H
    sin, cos = np.sin(angle) / np.sqrt(H), np.cos(angle) / np.sqrt(H)
    hf = np.concatenate([sin, cos, -sin], axis=1)
    wt = np.arange(WH)[None, :]

    def rows(kw):
        angle = 2 * np.pi * ((kw * wt) % W) / W
        c, s = 2 * np.cos(angle) / np.sqrt(W), 2 * np.sin(angle) / np.sqrt(W)
        return np.concatenate([c, -s]), np.concatenate([s, c])

    def v_rows(kw):
        angle = 2 * np.pi * ((kw * wt) % W) / W
        return (np.cos(angle) / 2 / np.sqrt(W),) * 2

    odd = [rows(2 * j + 1) for j in range(NP)]
    even = [v_rows(0)] + [rows(2 * j) for j in range(1, NP)] + [v_rows(WH)]
    wi = [np.concatenate([r[part] for r in group]) for part in (0, 1) for group in (odd, even)]
    every = np.concatenate([a, hf] + wi, axis=1)
    return np.ascontiguousarray(every, dtype=np.float32)


A0, HF0 = 0, 2 * KW
WI0 = HF0 + 3 * K
NCONST = WI0 + 4 * WH
WORK = 2316


def build(nc, x, w1r, w1i, b1r, b1i, w2r, w2i, b2r, b2i, consts, out):
    xv = x.rearrange("b h (j w) (n c) -> b n w h j c", j=2, c=C)
    ov = out.rearrange("b h (j w) (n c) -> b n w h j c", j=2, c=C)

    with ExitStack() as ctx:
        def sb(name, shape):
            return ctx.enter_context(nc.sbuf_tensor(name, shape, F32))

        def sem(name):
            return ctx.enter_context(nc.semaphore(name))

        X = sb("X", [128, H, 2, C])
        YZ = sb("YZ", [128, 2 * KW, C])
        const = sb("const", [128, NCONST])
        w1 = sb("w1", [C + 1, 3, C])
        w2 = sb("w2", [C + 1, 3, C])
        work = sb("work", [128, WORK])

        def piece(at, *shape):
            n = int(np.prod(shape))
            v = work[:, at:at + n]
            names = "abc"[:len(shape)]
            return v.rearrange(f"p ({' '.join(names)}) -> p {' '.join(names)}", **dict(zip(names, shape)))

        Xs = piece(0, SLOTS, 3, H)
        k1 = [Xs[0:C, s, 2] for s in range(SLOTS)]
        o1 = piece(768, SLOTS, 2, H)
        Yr = piece(1284, SLOTS, 2, C)
        PiS = piece(1668, SLOTS, 2 * K)
        res = piece(1928, SLOTS, 2, C)
        A1 = piece(0, SLOTS, 2, H)
        VS = piece(512, 4, K)
        EO = piece(772, 2, 2, H)
        fold = piece(1284, SLOTS, 2, H)
        folds = piece(1284, DEEP, 2, H)
        GC = piece(1796, 2, 2, K)
        GS = piece(2056, 2, 2, K)

        psum = [ctx.enter_context(nc.psum_tensor(f"ps{i}", [128, 512], F32)) for i in range(8)]
        P = psum[0:2]
        M1 = psum[2:4]
        M2 = psum[4:8]
        PG = psum[0:4]
        PU, PV = psum[5], psum[6]
        PU_last = psum[2]
        PA = (psum[7], psum[4])
        PA0 = psum[4:8]

        Acol = const[:, A0:A0 + 2 * KW]
        hf = const[:, HF0:HF0 + 3 * K]
        SC = hf[:, 0:2 * K]
        CnS = hf[:, K:3 * K]
        WIc, WIs = ([const[:, WI0 + (2 * part + g) * WH:WI0 + (2 * part + g + 1) * WH] for g in (0, 1)]
                    for part in (0, 1))

        def slots(first, step, n):
            return bass.AP(tensor=YZ[:].tensor, offset=first * C, ap=[[2 * KW * C, 128], [step * C, n], [1, C]])

        Z_rows = bass.AP(tensor=YZ[:].tensor, offset=0,
                         ap=[[2 * KW * C, 128], [(H + 1) * C, 2], [C, H], [1, C]])

        counted = {e: {n: sem(n) for n in names} for e, names in {
            "pe": ("h_done", "mix1_done", "mix2_done", "ih_done", "a_done", "u_done", "v_done"),
            "act": ("yr_ready", "pi_ready", "k1_ready", "o1_ready", "gc_ready", "gs_ready", "y_ready", "vs_ready"),
            "dve": ("xs_ready", "sum_ready", "hidden_ready", "clip_ready", "z_ready", "a1_ready", "eo_ready",
                    "out_ready", "half_ready", "half_added"),
            "pool": ("fold_ready", "row_added", "last_added"),
        }.items()}
        (h_done, mix1_done, mix2_done, ih_done, a_done, u_done, v_done) = counted["pe"].values()
        (yr_ready, pi_ready, k1_ready, o1_ready, gc_ready, gs_ready, y_ready, vs_ready) = counted["act"].values()
        (xs_ready, sum_ready, hidden_ready, clip_ready, z_ready, a1_ready, eo_ready,
         out_ready, half_ready, half_added) = counted["dve"].values()
        (fold_ready, row_added, last_added) = counted["pool"].values()
        merged = sem("merged")
        negated = sem("negated")
        weights_ready = sem("weights_ready")
        ones_ready = sem("ones_ready")
        pool_waits = sem("pool_waits")
        const_in = sem("const_in")
        weights_in = sem("weights_in")
        x_in = sem("x_in")
        res_in = [sem(f"res_in{i}") for i in range(SLOTS)]
        stored = [sem(f"stored{i}") for i in range(LAG)]
        WEIGHT_DMAS = 8
        MERGES = 5

        def made(n):
            return n + 1 + BIAS

        def freed(n):
            return n - SLOTS + 1 + BIAS

        def x_loads(u):
            return 16 * (2 * GROUPS + H // 2 * (u - 1))

        block = ctx.enter_context(nc.Block())

        @block.sync
        def _(sp):
            def load_weights(n):
                for dst, src in ((w1[0:C, 0, :], w1r[n]), (w1[0:C, 2, :], w1i[n]),
                                 (w2[0:C, 1, :], w2r[n]), (w2[0:C, 2, :], w2i[n]),
                                 (w1[C:C + 1, 1, :], b1r[n].rearrange("(a c) -> a c", a=1)),
                                 (w1[C:C + 1, 2, :], b1i[n].rearrange("(a c) -> a c", a=1)),
                                 (w2[C:C + 1, 1, :], b2r[n].rearrange("(a c) -> a c", a=1)),
                                 (w2[C:C + 1, 2, :], b2i[n].rearrange("(a c) -> a c", a=1))):
                    sp.dma_start(dst, src).then_inc(weights_in, 16)

            def load_unit(b, n):
                for g in range(GROUPS):
                    rows = slice(g * H // GROUPS, (g + 1) * H // GROUPS)
                    sp.dma_start(X[:, rows], xv[b, n][:, rows]).then_inc(x_in, 16)

            def finish_unit(v, b, n, nxt):
                def turn(i, d, load=True, store=True, replace=True):
                    p = LAG * i + d
                    if load:
                        for r in range(SLOTS):
                            sp.wait_ge(row_added, freed(H * v + 2 * p + r))
                            sp.dma_start(res[:, r], xv[b, n][:, bass.ds(2 * p + r, 1)].rearrange(
                                "w h j c -> w (h j) c")).then_inc(res_in[r], 16)
                    if store:
                        sp.wait_ge(row_added, made(H * v + 2 * p - 1))
                        rows = bass.ds(2 * p - 2, 2)
                        sp.dma_start(ov[b, n][:, rows], X[:, rows]).then_inc(stored[(d - 1) % LAG], 16)
                    if replace:
                        sp.wait_ge(stored[d], 16 * (H // 2 // LAG * v + i))
                        rows = bass.ds(2 * p - 2 * LAG, 2)
                        sp.dma_start(X[:, rows], xv[nxt[0], nxt[1]][:, rows]).then_inc(x_in, 16)

                sp.wait_ge(out_ready, made(PAIRS * v + PAIRS - 1))
                for d in range(LAG):
                    turn(0, d, store=d > 0, replace=False)
                with sp.Fori(1, H // 2 // LAG) as i:
                    for d in range(LAG):
                        turn(i, d)
                for d in range(LAG):
                    turn(H // 2 // LAG, d, load=False, store=d == 0)

            def next_weights(u, n):
                sp.wait_ge(mix2_done, made(T * u + T - 1))
                load_weights(n)

            sp.dma_start(const[:], consts).then_inc(const_in, 16)
            load_unit(0, 0)
            load_weights(0)
            sp.wait_ge(fold_ready, made(C - 1))
            load_unit(1, 0)
            next_weights(0, 0)
            with sp.Fori(0, NB - 1) as k:
                finish_unit(2 * k, 0, k, (0, k + 1))
                next_weights(2 * k + 1, k + 1)
                finish_unit(2 * k + 1, 1, k, (1, k + 1))
                next_weights(2 * k + 2, k + 1)
            finish_unit(UNITS - 2, 0, NB - 1, (1, NB - 1))
            sp.wait_ge(half_added, made(PAIRS - 1))
            sp.wait_ge(last_added, made(PAIRS - 1))
            for g in range(GROUPS):
                rows = slice(g * H // GROUPS, (g + 1) * H // GROUPS)
                sp.dma_start(ov[1, NB - 1][:, rows], X[:, rows]).then_inc(stored[g % LAG], 16)
            for s in range(LAG):
                sp.wait_ge(stored[s], 16 * (H // 2 // LAG * (UNITS - 1) + GROUPS // LAG))

        @block.tensor
        def _(pe):
            def h_sums(u, t, slot, mirrored=False):
                for_re, for_im = (SC, CnS) if mirrored else (CnS, SC)
                pe.wait_ge(yr_ready, made(T * u + t))
                pe.matmul(P[slot][0:C, 0:2 * K], Yr[:, slot, 0, :], for_re, start=True, stop=True)
                pe.matmul(P[slot][0:C, 2 * K:4 * K], Yr[:, slot, 1, :], for_im,
                          start=True, stop=True).then_inc(h_done, 1)

            def mix1(u, t, slot):
                m, xs = M1[slot][0:C], Xs[0:C + 1, slot]
                pe.wait_ge(sum_ready, made(T * u + t))
                pe.matmul(m[:, 0:H], w1[:, 1, :], xs[:, 1, :], start=True, stop=True)
                pe.matmul(m[:, H:2 * H], w1[:, 2, :], xs[:, 0, :], start=True, stop=True)
                pe.matmul(m[:, 2 * H:3 * H], w1[0:C, 0, :], xs[0:C, 2, :], start=True, stop=True).then_inc(mix1_done, 1)

            def mix2(u, t, slot):
                pe.wait_ge(o1_ready, made(T * u + t))
                m = M2[slot][:, 0:2 * C]
                pe.matmul(m, o1[0:C + 1, slot % 2, 0, :], w2[:, 1:3, :], start=True, stop=False)
                pe.matmul(m, o1[0:C, slot % 2, 1, :], w2[0:C, 0:2, :], start=False, stop=True).then_inc(mix2_done, 1)

            def phase1(u, forward=True):
                def step(t, q):
                    known, d = isinstance(t, int), q % 2
                    if not (known and t < 2):
                        pe.wait_ge(xs_ready, freed(T * u + t))
                    h_sums(u, t, d, mirrored=known and t in MIRRORED)
                    mixes(u, t, q)

                def mixes(u, t, q):
                    known, d = isinstance(t, int), q % 2
                    if not (known and t < 4):
                        if not (known and t < 8):
                            pe.wait_ge(z_ready, made(T * u + t - 8))
                        if known and t == 4:
                            pe.wait_ge(ones_ready, 2 * u + 2)
                        mix2(u, t - 4, q)
                    if known and t == 2:
                        pe.wait_ge(weights_ready, u + 1)
                        pe.wait_ge(ones_ready, 2 * u + 1)
                    if not (known and (t < 2 or t >= T + 2)):
                        pe.wait_ge(hidden_ready, freed(T * u + t - 2))
                        mix1(u, t - 2, d)

                for t in range(8):
                    step(t, t % 4)
                with pe.Fori(2, T // 4) as i:
                    for q in range(4):
                        step(4 * i + q, q)
                for t in range(T - T % 4, T):
                    step(t, t % 4)
                for t in range(T, T + 4):
                    mixes(u, t, t % 4)
                    if forward and t >= T + 2:
                        a_forward(u + 1, t - T - 2, t - T - 2)

            def ih(u, c, q):
                pe.wait_ge(a1_ready, made(C * u + c))
                if not (isinstance(c, int) and c < 4):
                    pe.wait_ge(gc_ready, made(C * u + c - 4))
                for g in range(2):
                    last = pe.matmul(PG[q][:, g * 2 * K:(g + 1) * 2 * K], A1[:, q % 2, g, :], CnS,
                                     start=True, stop=True)
                last.then_inc(ih_done, 1)

            def transform(y, o_e):
                pe.matmul(y[:, 0:H], o_e[:, 0, :], Acol[:, 0:H], start=True, stop=True)
                pe.matmul(y[:, H:2 * KW], o_e[:, 1, :], Acol[:, H:2 * KW], start=True, stop=True).then_inc(a_done, 1)

            def a_first(c, slot):
                pe.wait_ge(fold_ready, made(c))
                if not (isinstance(c, int) and c < DEEP):
                    pe.wait_ge(y_ready, made(c - DEEP))
                transform(PA0[slot], folds[:, slot])

            def a_forward(u, c, slot):
                pe.wait_ge(fold_ready, made(C * u + c))
                pe.wait_ge(y_ready, freed(C * u + c))
                if isinstance(c, int) and c < SLOTS:
                    pe.wait_ge(z_ready, made(T * u + c - 4))
                transform(PA[slot], fold[:, slot])

            def iw_s(u, p):
                pe.wait_ge(gs_ready, made(C * u + 2 * p + 1))
                pe.wait_ge(vs_ready, made(PAIRS * u + p - 1))
                for g in range(2):
                    last = pe.matmul(PV[:, g * 2 * K:(g + 1) * 2 * K], WIs[g], GS[:, g], start=True, stop=True)
                last.then_inc(v_done, 1)

            def iw_c(u, p, bank=PU):
                pe.wait_ge(gc_ready, made(C * u + 2 * p + 1))
                if bank is PU:
                    pe.wait_ge(eo_ready, made(PAIRS * u + p - 1))
                for g in range(2):
                    last = pe.matmul(bank[:, g * 2 * K:(g + 1) * 2 * K], WIc[g], GC[:, g], start=True, stop=True)
                last.then_inc(u_done, 1)

            def phase2(u, forward):
                def pair(p, e, first=False):
                    for d in range(2):
                        ih(u, 2 * p + d, 2 * e + d)
                        if forward and not first:
                            a_forward(u + 1, 2 * p + d, d)
                        if not first:
                            (iw_s, iw_c)[d](u, p - 1)

                pair(0, 0, first=True)
                pair(1, 1)
                with pe.Fori(1, PAIRS // 2) as i:
                    pair(2 * i, 0)
                    pair(2 * i + 1, 1)
                iw_s(u, PAIRS - 1)
                iw_c(u, PAIRS - 1, PU_last)

            for s in counted["pe"].values():
                pe.sem_inc(s, BIAS)
            pe.wait_ge(const_in, 16)
            for c in range(DEEP):
                a_first(c, c)
            with pe.Fori(1, C // DEEP) as i:
                for d in range(DEEP):
                    a_first(DEEP * i + d, d)
            phase1(0)
            phase2(0, True)
            with pe.Fori(1, UNITS - 1) as u:
                phase1(u)
                phase2(u, True)
            phase1(UNITS - 1, False)
            phase2(UNITS - 1, False)

        @block.scalar
        def _(act):
            Y = YZ[:].rearrange("p (k a) c -> p k a c", a=2)

            def copy_pi(u, t, slot):
                act.wait_ge(h_done, made(T * u + t))
                act.activation(PiS[0:C, slot], P[slot][0:C, 2 * K:4 * K], ACT.Copy).then_inc(pi_ready, 1)

            def copy_k1(u, t, slot):
                act.wait_ge(mix1_done, made(T * u + t))
                act.activation(k1[slot], M1[slot][0:C, 2 * H:3 * H], ACT.Copy).then_inc(k1_ready, 1)

            def relu(u, t, slot):
                act.wait_ge(hidden_ready, made(T * u + t))
                act.activation(o1[0:C, slot], o1[0:C, slot], ACT.Relu).then_inc(o1_ready, 1)

            def copy_yr(u, t, slot, k):
                act.activation(Yr[:, slot], Y[:, bass.ds(k, 1)].rearrange("p k a c -> p (k a) c"),
                               ACT.Copy).then_inc(yr_ready, 1)

            def phase1(u):
                act.wait_ge(y_ready, made(C * u + C - 1))
                copy_yr(u, 0, 0, NP)
                copy_yr(u, 1, 1, NP)

                def step(t, d, k):
                    act.wait_ge(xs_ready, freed(T * u + t))
                    copy_pi(u, t, d)
                    if k is not None:
                        act.wait_ge(h_done, freed(T * u + t + 1))
                        copy_yr(u, t + 1, 1 - d, k)
                    if not (isinstance(t, int) and t < 3):
                        relu(u, t - 3, 1 - d)
                    if not (isinstance(t, int) and t < 2):
                        copy_k1(u, t - 2, d)

                step(0, 0, None)
                step(1, 1, 2 * NP)
                step(2, 0, 2 * NP)
                step(3, 1, 0)
                with act.Fori(0, (NP - 1) // 3) as j:
                    for i in (3 * j, 3 * j + 1, 3 * j + 2):
                        step(2 * i + 4, 0, NP + 1 + i)
                        step(2 * i + 5, 1, i + 1)
                step(T - 1, 0, None)
                for t in (T - 2, T - 1):
                    relu(u, t - 1, (t - 1) % 2)
                    copy_k1(u, t, t % 2)
                relu(u, T - 1, (T - 1) % 2)

            def copy_y(u, c, bank):
                act.wait_ge(a_done, made(C * u + c))
                act.activation(YZ[:, :, bass.ds(c, 1)], bank[:, 0:2 * KW].rearrange("p (n a) -> p n a", a=1),
                               ACT.Copy).then_inc(y_ready, 1)

            def copy_g(u, p, c, q, part):
                G, ready, used = ((GC, gc_ready, u_done), (GS, gs_ready, v_done))[part]
                act.wait_ge(ih_done, made(C * u + c))
                if q % 2 == 0:
                    act.wait_ge(used, made(PAIRS * u + p - 1))
                sums = PG[q][:, 0:4 * K].rearrange("p (g a k) -> p g a k", g=2, a=2)
                act.activation(G[:, :, q % 2, :], sums[:, :, part, :], ACT.Copy).then_inc(ready, 1)

            def copy_v(u, p):
                act.wait_ge(v_done, made(PAIRS * u + p))
                act.wait_ge(eo_ready, made(PAIRS * u + p - 1))
                act.activation(VS, PV[:, 0:4 * K].rearrange("p (a k) -> p a k", a=4), ACT.Copy).then_inc(vs_ready, 1)

            def phase2(u, forward):
                act.wait_ge(row_added, H * u + BIAS)

                def pair(p, e, first=False):
                    c, q = 2 * p, 2 * e
                    if forward:
                        act.wait_ge(a1_ready, made(C * u + c))
                        copy_y(u + 1, c, PA[0])
                    if not first:
                        copy_v(u, p - 1)
                    copy_g(u, p, c, q, 1)
                    copy_g(u, p, c + 1, q + 1, 1)
                    if forward:
                        act.wait_ge(a1_ready, made(C * u + c + 1))
                        copy_y(u + 1, c + 1, PA[1])
                    copy_g(u, p, c, q, 0)
                    copy_g(u, p, c + 1, q + 1, 0)

                pair(0, 0, first=True)
                pair(1, 1)
                with act.Fori(1, PAIRS // 2) as i:
                    pair(2 * i, 0)
                    pair(2 * i + 1, 1)
                copy_v(u, PAIRS - 1)

            for s in counted["act"].values():
                act.sem_inc(s, BIAS)
            for c in range(DEEP):
                copy_y(0, c, PA0[c])
            with act.Fori(1, C // DEEP) as i:
                for d in range(DEEP):
                    copy_y(0, DEEP * i + d, PA0[d])
            phase1(0)
            phase2(0, True)
            with act.Fori(1, UNITS - 1) as u:
                phase1(u)
                phase2(u, True)
            phase1(UNITS - 1)
            phase2(UNITS - 1, False)

        @block.vector
        def _(dve):
            def combine(u, t, slot, mirrored=False):
                re, im = (1, 0) if mirrored else (0, 1)
                dve.wait_ge(pi_ready, made(T * u + t))
                pr, pi, xs = P[slot][0:C, 0:2 * K], PiS[0:C, slot], Xs[0:C, slot]
                plus = xs[:, 1::-1, 0:K] if mirrored else xs[:, 0:2, 0:K]
                dve.tensor_tensor(plus, pr.rearrange("p (a k) -> p a k", a=2),
                                  pi.rearrange("p (a k) -> p a k", a=2), ALU.add)
                r, i = (slice(a * K + KM, a * K, -1) for a in (re, im))
                dve.tensor_tensor(xs[:, 0, K:H], pr[:, r], pi[:, r], ALU.subtract)
                dve.tensor_tensor(xs[:, 1, K:H], pi[:, i], pr[:, i], ALU.subtract).then_inc(xs_ready, 1)

            def add_parts(u, t, slot):
                dve.wait_ge(xs_ready, made(T * u + t))
                if not (isinstance(t, int) and t < 2):
                    dve.wait_ge(hidden_ready, made(T * u + t - 2))
                dve.tensor_tensor(Xs[0:C, slot, 2], Xs[0:C, slot, 0], Xs[0:C, slot, 1],
                                  ALU.add).then_inc(sum_ready, 1)

            def hidden(u, t, slot):
                dve.wait_ge(mix2_done, freed(T * u + t))
                dve.wait_ge(k1_ready, made(T * u + t))
                m = M1[slot][0:C, 0:2 * H].rearrange("p (a k) -> p a k", a=2)
                both = bass.AP(tensor=work[:].tensor, offset=k1[slot].offset, ap=[[WORK, C], [0, 2], [1, H]])
                dve.tensor_tensor(o1[0:C, slot], m, both, ALU.add).then_inc(hidden_ready, 1)

            def clip(u, t, m, z):
                dve.wait_ge(mix2_done, made(T * u + t))
                dve.tensor_scalar(z, m, LAMBDA, -LAMBDA, ALU.min, ALU.max).then_inc(clip_ready, 1)

            def shrink(u, t, m, z):
                dve.wait_ge(clip_ready, made(T * u + t))
                dve.tensor_tensor(z, m, z, ALU.subtract).then_inc(z_ready, 1)

            def prepare(u):
                dve.wait_ge(weights_in, 16 * WEIGHT_DMAS * (u + 1))
                dve.scalar_tensor_tensor(out=w1[0:C, 1, :], in0=w1[0:C, 2, :], scalar=-1.0, in1=w1[0:C, 0, :],
                                         op0=ALU.mult, op1=ALU.subtract).then_inc(negated, 1)
                dve.wait_ge(negated, u + 1)
                dve.tensor_tensor(w1[0:C, 2, :], w1[0:C, 2, :], w1[0:C, 0, :], ALU.subtract)
                dve.tensor_scalar(w2[0:C, 0, :], w2[0:C, 2, :], -1.0, None, ALU.mult).then_inc(weights_ready, 1)

            mix2_out = [m[:, 0:2 * C].rearrange("p (a c) -> p a c", a=2) for m in M2]
            Z = YZ[:].rearrange("p (k a) c -> p k a c", a=2)

            def z_of(j, d):
                return Z[:, bass.ds(d * (NP + 1) + j, 1)].rearrange("p k a c -> p (k a) c")

            def wait_merged(u, n):
                dve.wait_ge(merged, MERGES * u + n)

            def special(u, s):
                m = mix2_out[s]
                at0, at1 = 2 * NP, 4 * NP
                re0, im0 = slots(at0, 1, 1), slots(at0 + 1, 1, 1)
                re1, im1 = slots(at1, 1, 1), slots(at1 + 1, 1, 1)
                if s == 0:
                    z = slots(at0, 1, 2)
                elif s == 1:
                    z = slots(at1, 1, 2)
                elif s == 2:
                    wait_merged(u, 2)
                    z = slots(at1, 1, 2)
                else:
                    dve.wait_ge(z_ready, made(T * u + 2))
                    dve.tensor_tensor(re1, re1, im1, ALU.add).then_inc(merged, 1)
                    wait_merged(u, 3)
                    z = slots(at0, at1 + 1 - at0, 2)
                clip(u, s, m, z)
                shrink(u, s, m, z)
                if s == 1:
                    dve.wait_ge(z_ready, made(T * u + 1))
                    dve.tensor_tensor(im0, re0, im0, ALU.add)
                    dve.tensor_tensor(re1, re1, im1, ALU.subtract).then_inc(merged, 1)
                    wait_merged(u, 1)
                    dve.tensor_tensor(im0, im0, re1, ALU.add).then_inc(merged, 1)
                elif s == 3:
                    dve.wait_ge(z_ready, made(T * u + 3))
                    dve.tensor_tensor(re0, re0, im1, ALU.subtract).then_inc(merged, 1)
                    wait_merged(u, 4)
                    dve.tensor_tensor(re1, re1, re0, ALU.add).then_inc(merged, 1)

            def phase1(u):
                def step(t, q, i=None):
                    known, d = isinstance(t, int), q % 2
                    if i is not None:
                        clip(u, t - 4, mix2_out[q], z_of(i, d))
                    dve.wait_ge(mix1_done, freed(T * u + t))
                    combine(u, t, d, mirrored=known and t in MIRRORED)
                    if known and t == 0 and not (isinstance(u, int) and u == 0):
                        write_out(u - 1, PAIRS - 1, True)
                    if known and t == 2:
                        dve.wait_ge(out_ready, made(PAIRS * u - 1))
                    if not (known and t < 2):
                        hidden(u, t - 2, d)
                    if i is not None:
                        shrink(u, t - 4, mix2_out[q], z_of(i, d))
                    elif t >= 4:
                        special(u, t - 4)
                    add_parts(u, t, d)

                for t in range(8):
                    step(t, t % 4)
                with dve.Fori(0, (T - 8) // 4) as j:
                    for e in range(2):
                        for d in range(2):
                            step(4 * j + 2 * e + d + 8, 2 * e + d, 2 * j + e)
                for t in range(T - T % 4, T):
                    step(t, t % 4, (t - 8) // 2)
                for t in range(T - 4, T):
                    z = z_of((t - 4) // 2, t % 2)
                    clip(u, t, mix2_out[t % 4], z)
                    shrink(u, t, mix2_out[t % 4], z)
                    if t + 2 < T:
                        hidden(u, t + 2, t % 2)

            def gather(u, c, slot):
                dve.tensor_copy(A1[:, slot], Z_rows[:, :, :, bass.ds(c, 1)].rearrange(
                    "p g n a -> p g (n a)")).then_inc(a1_ready, 1)

            def halves(u, p, bank=PU):
                uv = bank[:, 0:4 * K].rearrange("p (a k) -> p a k", a=4)
                eo = EO.rearrange("p a c h -> p (a c) h")
                dve.wait_ge(u_done, made(PAIRS * u + p))
                dve.wait_ge(vs_ready, made(PAIRS * u + p))
                dve.wait_ge(out_ready, made(PAIRS * u + p - 1))
                dve.tensor_tensor(eo[:, :, 0:K], uv, VS, ALU.add)
                dve.tensor_tensor(eo[:, :, K:H], uv[:, :, KM:0:-1], VS[:, :, KM:0:-1],
                                  ALU.subtract).then_inc(eo_ready, 1)

            def write_out(u, p, forward):
                place = [X[:, :, j, bass.ds(2 * p, 2)].rearrange("p h c -> p c h") for j in (0, 1)]
                dve.wait_ge(eo_ready, made(PAIRS * u + p))
                if forward:
                    dve.wait_ge(fold_ready, made(C * (u + 1) + 2 * p + 1))
                    dve.tensor_tensor(place[0], EO[:, 1], EO[:, 0], ALU.add)
                    dve.tensor_tensor(place[1], EO[:, 1], EO[:, 0], ALU.subtract).then_inc(out_ready, 1)
                else:
                    dve.wait_ge(half_added, made(p - 1))
                    dve.tensor_tensor(fold[:, 0], EO[:, 1], EO[:, 0], ALU.add).then_inc(half_ready, 1)
                    dve.wait_ge(last_added, made(p - 1))
                    dve.tensor_tensor(fold[:, 1], EO[:, 1], EO[:, 0], ALU.subtract).then_inc(out_ready, 1)
                    dve.wait_ge(x_in, x_loads(UNITS))
                    dve.wait_ge(half_ready, made(p))
                    dve.tensor_tensor(place[0], place[0], fold[:, 0], ALU.add).then_inc(half_added, 1)

            def phase2(u, forward):
                dve.wait_ge(z_ready, made(T * u + T - 1))
                wait_merged(u, MERGES)
                gather(u, 0, 0)
                gather(u, 1, 1)

                def pair(p):
                    known = isinstance(p, int)
                    dve.wait_ge(ih_done, freed(C * u + 2 * p))
                    gather(u, 2 * p, 0)
                    if not (known and p < 3):
                        write_out(u, p - 3, forward)
                    dve.wait_ge(ih_done, freed(C * u + 2 * p + 1))
                    gather(u, 2 * p + 1, 1)
                    if not (known and p < 2):
                        halves(u, p - 2)

                pair(1)
                pair(2)
                pair(3)
                with dve.Fori(2, PAIRS // 2) as i:
                    pair(2 * i)
                    pair(2 * i + 1)
                write_out(u, PAIRS - 3, forward)
                if forward:
                    prepare(u + 1)
                halves(u, PAIRS - 2)
                write_out(u, PAIRS - 2, forward)
                halves(u, PAIRS - 1, PU_last)
                if not forward:
                    write_out(u, PAIRS - 1, forward)

            def fold_first(c, slot):
                if not (isinstance(c, int) and c < DEEP):
                    dve.wait_ge(a_done, made(c - DEEP))
                lo, hi = (X[:, :, j, bass.ds(c, 1)].rearrange("p h a -> p (h a)") for j in (0, 1))
                dve.tensor_tensor(folds[:, slot, 0, :], lo, hi, ALU.subtract)
                dve.tensor_tensor(folds[:, slot, 1, :], lo, hi, ALU.add).then_inc(fold_ready, 1)

            for s in counted["dve"].values():
                dve.sem_inc(s, BIAS)
            dve.wait_ge(x_in, 16 * GROUPS)
            dve.wait_ge(fold_ready, BIAS)
            for c in range(DEEP):
                fold_first(c, c)
            with dve.Fori(1, C // DEEP) as i:
                for d in range(DEEP):
                    fold_first(DEEP * i + d, d)
            prepare(0)
            phase1(0)
            phase2(0, True)
            with dve.Fori(1, UNITS - 1) as u:
                phase1(u)
                phase2(u, True)
            phase1(UNITS - 1)
            phase2(UNITS - 1, False)

        @block.gpsimd
        def _(pool):
            def alone():
                pool.sem_inc(pool_waits, 1)

            def add_rows(v, i):
                for d in range(2):
                    pool.wait_ge(res_in[d], 16 * (H // 2 * v + i + 1))
                    row = X[:, bass.ds(2 * i + d, 1)].rearrange("p h j c -> p (h j) c")
                    pool.tensor_tensor(row, row, res[:, d], ALU.add).then_inc(row_added, 1)

            def ones(u):
                pool.wait_ge(eo_ready, made(PAIRS * u - 1))
                alone()
                pool.memset(Xs[C:C + 1, :, 0:2, :], 1.0).then_inc(ones_ready, 1)
                pool.wait_ge(out_ready, made(PAIRS * u - 1))
                alone()
                pool.memset(o1[C:C + 1, :, 0, :], 1.0).then_inc(ones_ready, 1)
                pool.wait_ge(ones_ready, 2 * u + 2)
                alone()

            def add_unit(v):
                with pool.Fori(0, H // 4) as i:
                    add_rows(v, 2 * i)
                    add_rows(v, 2 * i + 1)

            def fold_channel(u, c, slot):
                pool.wait_ge(a_done, freed(C * u + c))
                lo, hi = (X[:, :, j, bass.ds(c, 1)].rearrange("p h a -> p (h a)") for j in (0, 1))
                pool.tensor_tensor(fold[:, slot, 0, :], lo, hi, ALU.subtract)
                pool.tensor_tensor(fold[:, slot, 1, :], lo, hi, ALU.add).then_inc(fold_ready, 1)

            def fold_unit(u):
                pool.wait_ge(xs_ready, made(T * (u - 1) + T - 1))
                alone()
                pool.wait_ge(x_in, x_loads(u))
                alone()
                with pool.Fori(0, C // 4) as i:
                    for d in range(4):
                        fold_channel(u, 4 * i + d, d % 2)

            def add_last(p):
                pool.wait_ge(out_ready, made(PAIRS * (UNITS - 1) + p))
                xc = X[:, :, 1, bass.ds(2 * p, 2)].rearrange("p h c -> p c h")
                pool.tensor_tensor(xc, xc, fold[:, 1], ALU.add).then_inc(last_added, 1)

            for s in counted["pool"].values():
                pool.sem_inc(s, BIAS)
            ones(0)
            fold_unit(1)
            with pool.Fori(1, UNITS - 1) as u:
                ones(u)
                add_unit(u - 1)
                fold_unit(u + 1)
            ones(UNITS - 1)
            add_unit(UNITS - 2)
            pool.wait_ge(x_in, x_loads(UNITS))
            with pool.Fori(0, PAIRS // 2) as i:
                add_last(2 * i)
                add_last(2 * i + 1)


def kernel(x, L0_conv_w1r, L0_conv_w1i, L0_conv_b1r, L0_conv_b1i,
           L0_conv_w2r, L0_conv_w2i, L0_conv_b2r, L0_conv_b2i):
    import concourse.bacc as bacc
    from concourse.bass_utils import run_bass_kernel_spmd

    nc = bacc.Bacc("TRN2", target_bir_lowering=False, num_devices=1)
    arrays = {
        "x": x, "w1r": L0_conv_w1r, "w1i": L0_conv_w1i, "b1r": L0_conv_b1r, "b1i": L0_conv_b1i,
        "w2r": L0_conv_w2r, "w2i": L0_conv_w2i, "b2r": L0_conv_b2r, "b2i": L0_conv_b2i,
        "consts": dft_constants(),
    }
    arrays = {f"in_{k}": np.ascontiguousarray(v) for k, v in arrays.items()}
    args = [nc.dram_tensor(k, v.shape, F32, kind="ExternalInput").ap() for k, v in arrays.items()]
    out = nc.dram_tensor("out", (B, H, W, D), F32, kind="ExternalOutput").ap()
    build(nc, *args, out)
    r = run_bass_kernel_spmd(nc, [arrays], core_ids=[0])
    return r.results[0]["out"]
```
